# Optimizing a Trainium2 kernel written in Bass

```python
import numpy as np
import jax
import jax.numpy as jnp

def _softmax(x, axis=-1):
    return jax.nn.softmax(x, axis=axis)

def _gelu(x):
    return jax.nn.gelu(x, approximate=True)

def _silu(x):
    return jax.nn.silu(x)

def _sigmoid(x):
    return jax.nn.sigmoid(x)

def _layernorm(x, axis=-1, eps=1e-05):
    m = jnp.mean(x, axis=axis, keepdims=True)
    v = jnp.var(x, axis=axis, keepdims=True)
    return (x - m) / jnp.sqrt(v + eps)

def _scatter_add(tgt, idx, src, axis=0):
    return tgt.at[idx].add(src)

def _segment_sum(src, seg, n):
    return jax.ops.segment_sum(src, seg, n)
kernel_name = 'mk_adj_seq_d1_adj_r2_2829be'

def setup_inputs(seed: int=0):
    np.random.seed(seed)
    _w = jnp.asarray

    def _rec_inputs():
        import jax
        import jax.numpy as jnp
        _gk = jax.random.key(seed)
        x = 7.22e-05 + 1 * jax.random.normal(jax.random.fold_in(_gk, 1), (8, 1024, 256), jnp.float32)
        _a = jax.random.bernoulli(jax.random.fold_in(_gk, 2), 0.00390625, (8, 1024, 1024))
        adj = _a.astype(jnp.int32)
        return (x, adj)
    x, adj = _rec_inputs()

    def _L0_gnn_setup():
        import jax, jax.numpy as jnp
        import numpy as np
        B, N, E, FF, L = (8, 1024, 256, 128, 2)
        LN_EPS = 1e-05
        SCALE = float(np.sqrt(FF))

        def layer_norm(x, g, b):
            m = jnp.mean(x, axis=-1, keepdims=True)
            v = jnp.mean(jnp.square(x - m), axis=-1, keepdims=True)
            return (x - m) * jax.lax.rsqrt(v + LN_EPS) * g + b
        key = jax.random.key(seed)
        ks = jax.random.split(key, 9)
        s = 0.02
        node_fts = jax.random.normal(ks[0], (B, N, E), jnp.float32)
        rel_edges = jax.random.randint(ks[1], (B, N, N), 0, 2, jnp.int32)
        Wq = jax.random.normal(ks[2], (L, FF, E), jnp.float32) * s
        bq = jnp.zeros((L, FF), jnp.float32)
        Wk = jax.random.normal(ks[3], (L, FF, E), jnp.float32) * s
        bk = jnp.zeros((L, FF), jnp.float32)
        Wc = jax.random.normal(ks[4], (L, E, E), jnp.float32) * s
        ln_g = jnp.ones((L, E), jnp.float32)
        ln_b = jnp.zeros((L, E), jnp.float32)
        return {'node_fts': node_fts, 'rel_edges': rel_edges, 'Wq': Wq, 'bq': bq, 'Wk': Wk, 'bk': bk, 'Wc': Wc, 'ln_g': ln_g, 'ln_b': ln_b}
    _L0_gnn_all = _L0_gnn_setup()
    _L0_gnn_in = {k: v for k, v in _L0_gnn_all.items() if k in ('Wq', 'bq', 'Wk', 'bk', 'Wc', 'ln_g', 'ln_b')}
    del _L0_gnn_all
    return {'x': x, 'adj': adj, 'L0_gnn_Wq': _L0_gnn_in['Wq'], 'L0_gnn_bq': _L0_gnn_in['bq'], 'L0_gnn_Wk': _L0_gnn_in['Wk'], 'L0_gnn_bk': _L0_gnn_in['bk'], 'L0_gnn_Wc': _L0_gnn_in['Wc'], 'L0_gnn_ln_g': _L0_gnn_in['ln_g'], 'L0_gnn_ln_b': _L0_gnn_in['ln_b']}

def reference(x, adj, L0_gnn_Wq, L0_gnn_bq, L0_gnn_Wk, L0_gnn_bk, L0_gnn_Wc, L0_gnn_ln_g, L0_gnn_ln_b):
    import jax
    import jax.numpy as jnp

    def _L0_gnn_ref(node_fts, rel_edges, Wq, bq, Wk, bk, Wc, ln_g, ln_b):
        import jax, jax.numpy as jnp
        import numpy as np
        B, N, E, FF, L = (8, 1024, 256, 128, 2)
        LN_EPS = 1e-05
        SCALE = float(np.sqrt(FF))

        def layer_norm(x, g, b):
            m = jnp.mean(x, axis=-1, keepdims=True)
            v = jnp.mean(jnp.square(x - m), axis=-1, keepdims=True)
            return (x - m) * jax.lax.rsqrt(v + LN_EPS) * g + b
        x = node_fts
        mask = rel_edges == 0
        for k in range(L):
            q = jnp.einsum('bnd,fd->bnf', x, Wq[k]) + bq[k]
            kk = jnp.einsum('bnd,fd->bnf', x, Wk[k]) + bk[k]
            scores = jnp.einsum('bof,bif->boi', q, kk) / SCALE
            scores = jnp.where(mask, -10000000000.0, scores)
            attn = jax.nn.softmax(scores, axis=2)
            attn = jnp.where(mask, 0.0, attn)
            ctx = jnp.einsum('boi,bid->bod', attn, x)
            ctx = jnp.einsum('bnd,ed->bne', ctx, Wc[k])
            x = layer_norm(x + ctx, ln_g[k], ln_b[k])
        return x
    x = _L0_gnn_ref(x, adj, L0_gnn_Wq, L0_gnn_bq, L0_gnn_Wk, L0_gnn_bk, L0_gnn_Wc, L0_gnn_ln_g, L0_gnn_ln_b)
    return x

_drawn_inputs = setup_inputs


def setup_inputs(seed=0):
    import zlib

    import numpy as np

    out = dict(_drawn_inputs(seed))
    spreads = {'L0_gnn_bq': (0.0, 0.8),
     'L0_gnn_bk': (0.0, 0.8),
     'L0_gnn_ln_g': (1.0, 0.2),
     'L0_gnn_ln_b': (0.0, 0.1)}
    factors = {'L0_gnn_Wq': 2.953, 'L0_gnn_Wk': 2.811}
    for name, (base, spread) in spreads.items():
        noise = np.random.default_rng([zlib.crc32(name.encode()), seed]).standard_normal(out[name].shape)
        drawn = base * np.exp(spread * noise) if base else spread * noise
        out[name] = jnp.asarray(drawn.astype(out[name].dtype))
    for name, factor in factors.items():
        out[name] = (out[name] * factor).astype(out[name].dtype)
    return out
```

```python
import concourse.bass as bass
from concourse import mybir
from contextlib import ExitStack


def gnn_kernel(nc, x, adj, wq, bq, wk, bk, wc, ln_g, ln_b, out):
    fp32 = mybir.dt.float32
    fp32r = mybir.dt.float32r
    bf16 = mybir.dt.bfloat16
    int32 = mybir.dt.int32
    ALU = mybir.AluOpType
    ACT = mybir.ActivationFunctionType

    P = 128
    NG, N, D = x.shape
    L, F, _ = wq.shape
    TILES = N // P
    DT = D // P
    PAIRS = NG // 2
    HALF = N // 2
    BANK = 512
    STAGES = 2 * L
    STEPS = STAGES * TILES
    EPS = 1e-5
    PENALTY = -1e30
    SCALE = float(F) ** 0.5
    NO_EDGE = -PENALTY / SCALE / 2

    SCHEDULE = [[("xT", 0)], [("xT", 1)], [("q", 0), ("k", 0)], [("xT", 2), ("z", 0)],
                [("z", 1)], [("xT", 3), ("z", 2)], [("q", 1), ("k", 1)], [("z", 3)]]
    ORDER = [group for step in SCHEDULE for group in step]
    GROUPS = len(ORDER)
    FIRST_ORDER = [("xT", 0), ("xT", 1), ("xT", 2), ("xT", 3), ("q", 0), ("k", 0), ("k", 1), ("q", 1),
                   ("z", 0), ("z", 1), ("z", 2), ("z", 3)]
    AHEAD = 8
    W_GROUPS = 2 * L
    ADJ_RING = 4
    RING = 4

    x_v = x.rearrange("g (j a p) d -> g j p a d", p=P, a=2)
    out_v = out.rearrange("g (j a p) d -> g j p a d", p=P, a=2)
    adj_v = adj.rearrange("g (t p) i -> g t p i", p=P)

    ctx = ExitStack()
    with ctx:
        def sb(name, shape, dt=fp32):
            return ctx.enter_context(nc.sbuf_tensor(name, shape, dt))

        def pb(name, shape):
            return ctx.enter_context(nc.psum_tensor(name, shape, fp32))

        def sem(name):
            return ctx.enter_context(nc.semaphore(name))

        def split(name, shape):
            return sb(name + "_high", shape, fp32r), sb(name + "_low", shape, fp32r)

        ident = sb("ident", [P, P])
        wq_in = sb("wq_in", [P, L, D])
        wk_in = sb("wk_in", [P, L, D])
        wc_in = sb("wc_in", [P, L, DT, D])
        bq_sb = sb("bq_sb", [P, L])
        bk_sb = sb("bk_sb", [P, L])
        gain = sb("gain", [P, L, D])
        shift = sb("shift", [P, L, D])
        minus_half = sb("minus_half", [P, 1])
        eps = sb("eps", [P, 1])
        wqk = [split(f"wqk{k}", [P, 2, DT, F]) for k in range(L)]
        wcT = [split(f"wcT{k}", [P, DT, D]) for k in range(L)]
        nodes = [sb(f"nodes{s}", [P, TILES, D]) for s in range(2)]
        penalty = [sb(f"penalty{s}", [P, TILES, N], bf16) for s in range(2)]
        adj_in = sb("adj_in", [P, ADJ_RING, N], int32)
        xT = split("xT", [P, DT, N])
        q = [split(f"q{s}", [P, N]) for s in range(2)]
        k = [split(f"k{s}", [P, N]) for s in range(2)]
        z = [split(f"z{s}", [P, TILES, D]) for s in range(2)]
        probs = [sb(f"probs{s}", [P, N]) for s in range(2)]
        pT = split("pT", [P, TILES, P])
        neg_max = sb("neg_max", [P, RING])
        row_sum = sb("row_sum", [P, RING])
        inverse = sb("inverse", [P, RING])
        weight = sb("weight", [P, RING])
        y = sb("y", [P, RING, D])
        stats = sb("stats", [P, RING, 6])
        moments = sb("moments", [P, RING, 2])
        var_eps = sb("var_eps", [P, 1])
        rstd = sb("rstd", [P, 1])
        normed = sb("normed", [P, D])
        centred = sb("centred", [P, D])

        scores_ps = pb("scores_ps", [P, N])
        pT_ps = pb("pT_ps", [P, N])
        ctx_ps = [pb(f"ctx_ps{s}", [P, BANK]) for s in range(2)]
        proj_ps = [pb(f"proj_ps{s}", [P, BANK]) for s in range(2)]

        wqk_arrived = sem("wqk_arrived")
        wc_arrived = sem("wc_arrived")
        vectors_in = sem("vectors_in")
        constants = sem("constants")
        x_in = [[sem(f"x_in{s}{j}") for j in range(TILES // 2)] for s in range(2)]
        stored = [[sem(f"stored{s}{j}") for j in range(TILES // 2)] for s in range(2)]
        adj_arrived = [sem(f"adj_arrived{r}") for r in range(ADJ_RING)]
        penalties = sem("penalties")
        proj_made = sem("proj_made")
        proj_high = sem("proj_high")
        proj_split = sem("proj_split")
        scores_made = sem("scores_made")
        masked = sem("masked")
        probs_made = sem("probs_made")
        pT_made = sem("pT_made")
        pT_high = sem("pT_high")
        pT_split = sem("pT_split")
        ctx_made = sem("ctx_made")
        inverted = sem("inverted")
        weighted = sem("weighted")
        y_made = sem("y_made")
        stats_made = sem("stats_made")
        moments_made = sem("moments_made")
        norm_step = sem("norm_step")
        nodes_made = sem("nodes_made")

        block = ctx.enter_context(nc.Block())

        def dest(group, s, part):
            kind, j = group
            if kind == "xT":
                return xT[part][:, :, 2 * P * j:2 * P * (j + 1)]
            if kind == "z":
                return z[s % 2][part][:, 2 * j:2 * j + 2, :]
            return {"q": q, "k": k}[kind][s % 2][part][:, HALF * j:HALF * (j + 1)]

        def bank(n):
            return proj_ps[n % 2]

        def bank_as(n, group):
            ps = bank(n)[:, :]
            return ps.rearrange("p (a c) -> p a c", a=2) if group[0] in ("xT", "z") else ps

        def first_group(p, s):
            return p * (STAGES * GROUPS) + (W_GROUPS + s * GROUPS)

        def place(s, group):
            return (FIRST_ORDER if s == 0 else ORDER).index(group)

        FIRST = range(TILES)
        BODY = range(TILES, STEPS + TILES)

        def exists(p, last, u):
            return u >= 0 and not (last and u >= STEPS)

        @block.sync
        def _(sp):
            def load_adj(graph, t, r):
                sp.dma_start(adj_in[:, r, :], adj_v[graph, t]).then_inc(adj_arrived[r], 16)

            def load_x(graph, s, j):
                sp.dma_start(nodes[s][:, 2 * j:2 * j + 2, :], x_v[graph, j]).then_inc(x_in[s][j], 16)

            def step(p, last, g):
                s, t = g // TILES, g % TILES
                for side in range(2):
                    j, odd = divmod(g - TILES * (2 + side) - 5, 2)
                    if odd == 0 and 0 <= j < TILES // 2:
                        sp.wait_ge(nodes_made, p * STEPS + (TILES * (2 + side) + 2 * j + 2))
                        sp.dma_start(out_v[p * 2 + side, j],
                                     nodes[side][:, 2 * j:2 * j + 2, :]).then_inc(stored[side][j], 16)
                    if odd == 1 and 0 <= j < TILES // 2 and not last:
                        sp.wait_ge(stored[side][j], p * 16 + 16)
                        load_x(p * 2 + (2 + side), side, j)
                if s == 4 and not last and t < ADJ_RING:
                    sp.wait_ge(penalties, p * 16 + (24 + t + 1))
                    load_adj(p * 2 + 3, ADJ_RING + t, t)
                if s == 1 and not last and t < ADJ_RING:
                    sp.wait_ge(penalties, p * 16 + (12 + t + 1))
                    load_adj(p * 2 + 2, t, t)
                if s == 3 and not last:
                    sp.wait_ge(penalties, p * 16 + (16 + t + 1))
                    load_adj(p * 2 + (2 if t < ADJ_RING else 3), (ADJ_RING + t) % TILES, t % ADJ_RING)

            for w_in, w in ((wq_in, wq), (wk_in, wk)):
                sp.dma_start(w_in[:, :, :], w.rearrange("l f d -> f l d")).then_inc(wqk_arrived, 16)
            for j in range(TILES // 2):
                load_x(0, 0, j)
            for layer in range(L):
                sp.dma_start(wc_in[:, layer], wc[layer].rearrange("(a p) d -> p a d", p=P)).then_inc(wc_arrived, 16)
            for t in range(ADJ_RING):
                load_adj(0, t, t)
            for j in range(TILES // 2):
                load_x(1, 1, j)
            for n in range(2 * TILES - ADJ_RING):
                sp.wait_ge(penalties, n + 1)
                load_adj((ADJ_RING + n) // TILES, (ADJ_RING + n) % TILES, n % ADJ_RING)
            for g in FIRST:
                step(0, False, g)
            with sp.Fori(0, PAIRS - 1) as p:
                for g in BODY:
                    step(p, False, g)
            for g in BODY:
                step(PAIRS - 1, True, g)
            for side in range(2):
                for j in range(TILES // 2):
                    sp.wait_ge(stored[side][j], 16 * PAIRS)

        @block.gpsimd
        def _(pool):
            nc.gpsimd.memset(minus_half[:, :], -0.5).then_inc(constants, 1)
            nc.gpsimd.memset(eps[:, :], EPS).then_inc(constants, 1)
            nc.gpsimd.memset(ident[:, :], 0.0).then_inc(constants, 1)
            pool.wait_ge(constants, 3)
            nc.gpsimd.affine_select(out=ident[:, :], in_=ident[:, :], compare_op=ALU.not_equal, fill=1.0,
                                    base=0, pattern=[[-1, P]], channel_multiplier=1).then_inc(constants, 1)
            with nc.allow_non_contiguous_dma(reason="a few bias values, once"):
                for b_sb, b in ((bq_sb, bq), (bk_sb, bk)):
                    pool.dma_start(b_sb[:, :], b.rearrange("l f -> f l")).then_inc(vectors_in, 16)
            for v_sb, v in ((gain, ln_g), (shift, ln_b)):
                pool.dma_start(v_sb[:, :, :], v[None, :, :].to_broadcast([P, L, D])).then_inc(vectors_in, 16)

            pool.wait_ge(vectors_in, 64)

            with pool.Fori(0, PAIRS) as p:
                for u in range(STEPS):
                    s, t = u // TILES, u % TILES
                    layer, r = s // 2, u % RING
                    done = p * (STEPS * 5) + 5 * u
                    pool.wait_ge(moments_made, p * STEPS + (u + 1))
                    nc.gpsimd.tensor_tensor(var_eps[:, :], moments[:, r, 1:2], eps[:, :],
                                            ALU.add).then_inc(norm_step, 1)
                    pool.wait_ge(norm_step, done + 1)
                    nc.gpsimd.tensor_tensor(rstd[:, :], var_eps[:, :], minus_half[:, :],
                                            ALU.pow).then_inc(norm_step, 1)
                    nc.gpsimd.tensor_tensor(centred[:, :], y[:, r, :], moments[:, r, 0:1].to_broadcast([P, D]),
                                            ALU.subtract).then_inc(norm_step, 1)
                    pool.wait_ge(norm_step, done + 3)
                    nc.gpsimd.tensor_tensor(normed[:, :], centred[:, :], rstd[:, :].to_broadcast([P, D]),
                                            ALU.mult).then_inc(norm_step, 1)
                    pool.wait_ge(norm_step, done + 4)
                    nc.gpsimd.tensor_tensor(centred[:, :], normed[:, :], gain[:, layer, :],
                                            ALU.mult).then_inc(norm_step, 1)
                    pool.wait_ge(norm_step, done + 5)
                    nc.gpsimd.tensor_tensor(nodes[s % 2][:, t, :], centred[:, :], shift[:, layer, :],
                                            ALU.add).then_inc(nodes_made, 1)

        @block.scalar
        def _(act):
            def proj_round(n, group, s, number):
                act.wait_ge(proj_made, number + 1)
                high = dest(group, s, 0)
                if group[0] in ("q", "k"):
                    bias = {"q": bq_sb, "k": bk_sb}[group[0]]
                    layer = s // 2 % L
                    nc.scalar.activation(high, bank_as(n, group), ACT.Identity,
                                         bias=bias[:, layer:layer + 1]).then_inc(proj_high, 1)
                else:
                    nc.scalar.activation(high, bank_as(n, group), ACT.Identity).then_inc(proj_high, 1)

            def projections(p, s, groups):
                for group in groups:
                    n = place(s, group)
                    proj_round(n, group, s, first_group(p, s) + n)

            def step(p, last, g):
                s, t = g // TILES, g % TILES
                u = g - 2
                if exists(p, last, u):
                    for h in range(2):
                        act.wait_ge(pT_made, p * (2 * STEPS) + (2 * u + h + 1))
                        nc.scalar.activation(pT[0][:, 4 * h:4 * h + 4, :],
                                             pT_ps[:, BANK * h:BANK * (h + 1)].rearrange("p (a c) -> p a c", c=P),
                                             ACT.Identity).then_inc(pT_high, 1)
                if exists(p, last, g):
                    r = g % RING
                    act.wait_ge(masked, p * STEPS + (g + 1))
                    nc.scalar.activation(probs[g % 2][:, :], probs[g % 2][:, :], ACT.Exp,
                                         bias=neg_max[:, r:r + 1], scale=-1.0,
                                         accum_out=row_sum[:, r:r + 1]).then_inc(probs_made, 1)
                if g == 0:
                    projections(p, 0, FIRST_ORDER[AHEAD:])
                if exists(p, last, g + TILES):
                    projections(p, s + 1, SCHEDULE[t])

            for w in range(W_GROUPS):
                act.wait_ge(proj_made, w + 1)
                high = wqk[w][0][:, :, :, :].rearrange("p a b c -> p (a b c)") if w < L else \
                    wcT[w - L][0][:, :, :].rearrange("p a b -> p (a b)")
                nc.scalar.activation(high, bank(w)[:, :], ACT.Identity).then_inc(proj_high, 1)
            act.wait_ge(vectors_in, 64)
            projections(0, 0, FIRST_ORDER[:AHEAD])
            for g in FIRST:
                step(0, False, g)
            with act.Fori(0, PAIRS - 1) as p:
                for g in BODY:
                    step(p, False, g)
            for g in BODY:
                step(PAIRS - 1, True, g)

        @block.vector
        def _(dve):
            def proj_rest(n, group, s, number):
                dve.wait_ge(proj_high, number + 1)
                high, low = dest(group, s, 0).bitcast(fp32), dest(group, s, 1)
                if group[0] in ("q", "k"):
                    bias = {"q": bq_sb, "k": bk_sb}[group[0]]
                    layer = s // 2 % L
                    nc.vector.scalar_tensor_tensor(out=low, in0=bank_as(n, group), scalar=bias[:, layer:layer + 1],
                                                   in1=high, op0=ALU.add, op1=ALU.subtract).then_inc(proj_split, 1)
                else:
                    nc.vector.tensor_tensor(low, bank_as(n, group), high, ALU.subtract).then_inc(proj_split, 1)

            def projections(p, s, groups):
                for group in groups:
                    n = place(s, group)
                    proj_rest(n, group, s, first_group(p, s) + n)

            def make_penalty(p, n):
                r = n % ADJ_RING
                dve.wait_ge(adj_arrived[r], p * 64 + 16 * (n // ADJ_RING + 1))
                nc.vector.tensor_scalar(penalty[n // TILES % 2][:, n % TILES, :], adj_in[:, r, :], 0.0, PENALTY,
                                        ALU.is_equal, ALU.mult).then_inc(penalties, 1)

            def step(p, last, g):
                s, t = g // TILES, g % TILES
                u = g - 3
                if exists(p, last, u):
                    r = u % RING
                    dve.wait_ge(ctx_made, p * STEPS + (u + 1))
                    dve.wait_ge(weighted, p * STEPS + (u + 1))
                    if u >= RING:
                        dve.wait_ge(nodes_made, p * STEPS + (u - RING + 1))
                    nc.vector.scalar_tensor_tensor(out=y[:, r, :], in0=ctx_ps[u % 2][:, 0:D],
                                                   scalar=weight[:, r:r + 1],
                                                   in1=nodes[u // TILES % 2][:, u % TILES, :],
                                                   op0=ALU.mult, op1=ALU.add).then_inc(y_made, 1)
                v = g - 2
                if exists(p, last, v):
                    for h in range(2):
                        dve.wait_ge(pT_high, p * (2 * STEPS) + (2 * v + h + 1))
                        nc.vector.tensor_tensor(pT[1][:, 4 * h:4 * h + 4, :],
                                                pT_ps[:, BANK * h:BANK * (h + 1)].rearrange("p (a c) -> p a c", c=P),
                                                pT[0][:, 4 * h:4 * h + 4, :].bitcast(fp32),
                                                ALU.subtract).then_inc(pT_split, 1)
                if exists(p, last, g):
                    if s == 0:
                        dve.wait_ge(penalties, t + 1)
                    elif t == 0 and s % STAGES < 2:
                        dve.wait_ge(penalties, p * 16 + (16 * (s // STAGES) + 8 * (s % STAGES + 1)))
                    dve.wait_ge(scores_made, p * STEPS + (g + 1))
                if exists(p, last, v):
                    r = v % RING
                    nc.vector.reciprocal(inverse[:, r:r + 1], row_sum[:, r:r + 1]).then_inc(inverted, 1)
                if exists(p, last, g):
                    r = g % RING
                    nc.vector.tensor_tensor_reduce(out=probs[g % 2][:, :], in0=scores_ps[:, :],
                                                   in1=penalty[s % 2][:, t, :], scale=-1.0 / SCALE, scalar=3e38,
                                                   op0=ALU.add, op1=ALU.min,
                                                   accum_out=neg_max[:, r:r + 1]).then_inc(masked, 1)
                if exists(p, last, v):
                    r = v % RING
                    dve.wait_ge(inverted, p * STEPS + (v + 1))
                    nc.vector.tensor_scalar(weight[:, r:r + 1], neg_max[:, r:r + 1], NO_EDGE,
                                            inverse[:, r:r + 1], ALU.is_lt, ALU.mult).then_inc(weighted, 1)
                if exists(p, last, u):
                    r = u % RING
                    dve.wait_ge(y_made, p * STEPS + (u + 1))
                    nc.vector.bn_stats(stats[:, r, :], y[:, r, :]).then_inc(stats_made, 1)
                if exists(p, last, u):
                    dve.wait_ge(stats_made, p * STEPS + (u + 1))
                if g == 0:
                    projections(p, 0, FIRST_ORDER[AHEAD:])
                if exists(p, last, g + TILES):
                    projections(p, s + 1, SCHEDULE[t])
                if exists(p, last, u):
                    r = u % RING
                    nc.vector.bn_aggr(moments[:, r, :], stats[:, r, :]).then_inc(moments_made, 1)
                if s == 0:
                    for n in range(2 + 2 * t, min(4 + 2 * t, 2 * TILES)):
                        make_penalty(p, n)
                if s in (3, 4) and not last:
                    make_penalty(p, 2 * TILES + TILES * (s - 3) + t)

            for w in range(W_GROUPS):
                dve.wait_ge(proj_high, w + 1)
                high, low = wqk[w] if w < L else wcT[w - L]
                if w < L:
                    high, low = (a[:, :, :, :].rearrange("p a b c -> p (a b c)") for a in (high, low))
                else:
                    high, low = (a[:, :, :].rearrange("p a b -> p (a b)") for a in (high, low))
                nc.vector.tensor_tensor(low, bank(w)[:, :], high.bitcast(fp32), ALU.subtract).then_inc(proj_split, 1)
            dve.wait_ge(vectors_in, 64)
            projections(0, 0, FIRST_ORDER[:AHEAD])
            for t in range(2):
                make_penalty(0, t)
            for g in FIRST:
                step(0, False, g)
            with dve.Fori(0, PAIRS - 1) as p:
                for g in BODY:
                    step(p, False, g)
            for g in BODY:
                step(PAIRS - 1, True, g)

        @block.tensor
        def _(pe):
            def product(ps, terms):
                for i, (a, b) in enumerate(terms):
                    last = nc.tensor.matmul(ps, a, b, start=i == 0, stop=i == len(terms) - 1)
                return last

            def three(high_low_a, high_low_b):
                (ah, al), (bh, bl) = high_low_a, high_low_b
                return [(ah, bh), (ah, bl), (al, bh)]

            def projection(p, s, group):
                kind, j = group
                n = place(s, group)
                number = first_group(p, s) + n
                layer, side = s // 2 % L, s % 2
                if kind == "xT":
                    if layer == 0:
                        pe.wait_ge(x_in[side][j], p * 16 + 16 * (s // STAGES + 1))
                    else:
                        pe.wait_ge(nodes_made, p * STEPS + (TILES * (s - 2) + 2 * j + 2))
                    pe.wait_ge(proj_split, number - 1)
                    ps = bank_as(n, group)
                    for a in range(2):
                        for d in range(DT):
                            last = nc.tensor.transpose(ps[:, d, a * P:(a + 1) * P],
                                                       nodes[side][:, 2 * j + a, d * P:(d + 1) * P], ident[:, :])
                    last.then_inc(proj_made, 1)
                    return
                needs = place(s, ("xT", j if kind == "z" else 2 * j + 1))
                pe.wait_ge(proj_split, number - n + max(n - 1, needs + 1))
                if kind == "z":
                    w = wcT[layer]
                    for a in range(2):
                        c = (2 * j + a) * P
                        last = product(bank(n)[:, a * D:(a + 1) * D],
                                       [pair for d in range(DT)
                                        for pair in three([xT[part][:, d, c:c + P] for part in range(2)],
                                                          [w[part][:, d, :] for part in range(2)])])
                else:
                    w, m = wqk[layer], 0 if kind == "q" else 1
                    last = product(bank(n)[:, :],
                                   [pair for d in range(DT)
                                    for pair in three([w[part][:, m, d, :] for part in range(2)],
                                                      [xT[part][:, d, HALF * j:HALF * (j + 1)]
                                                       for part in range(2)])])
                last.then_inc(proj_made, 1)

            def step(p, last, g):
                s, t = g // TILES, g % TILES
                side = s % 2
                if exists(p, last, g):
                    if t == 0:
                        pe.wait_ge(proj_split, first_group(p, s) + (max(place(s, ("k", 1)), place(s, ("q", 1))) + 1))
                    if g > 0:
                        pe.wait_ge(masked, p * STEPS + g)
                    rows = slice(t * P, (t + 1) * P)
                    (qh, ql), (kh, kl) = q[side], k[side]
                    halves = [(scores_ps[:, HALF * h:HALF * (h + 1)], slice(HALF * h, HALF * (h + 1)))
                              for h in range(2)]
                    for ps, cols in halves:
                        nc.tensor.matmul(ps, qh[:, rows], kh[:, cols], start=True, stop=False)
                        nc.tensor.matmul(ps, qh[:, rows], kl[:, cols], start=False, stop=False)
                    for ps, cols in halves:
                        done = nc.tensor.matmul(ps, ql[:, rows], kh[:, cols], start=False, stop=True)
                    done.then_inc(scores_made, 1)
                if g == 0:
                    for group in FIRST_ORDER[AHEAD:]:
                        projection(p, 0, group)
                if exists(p, last, g + TILES):
                    for group in SCHEDULE[t]:
                        projection(p, s + 1, group)
                u = g - 2
                if exists(p, last, u):
                    if u % TILES == 0:
                        pe.wait_ge(proj_split, first_group(p, u // TILES) + (place(u // TILES, ("z", 3)) + 1))
                    pe.wait_ge(pT_split, p * (2 * STEPS) + (2 * u + 2))
                    zz = z[u // TILES % 2]
                    product(ctx_ps[u % 2][:, 0:D],
                            [pair for i in range(TILES)
                             for pair in three([pT[part][:, i, :] for part in range(2)],
                                               [zz[part][:, i, :] for part in range(2)])]).then_inc(ctx_made, 1)
                v = g - 1
                if exists(p, last, v):
                    pe.wait_ge(probs_made, p * STEPS + (v + 1))
                    for i in range(TILES):
                        done = nc.tensor.transpose(pT_ps[:, i * P:(i + 1) * P],
                                                   probs[v % 2][:, i * P:(i + 1) * P], ident[:, :])
                        if i % 4 == 3:
                            done.then_inc(pT_made, 1)

            pe.wait_ge(constants, 4)
            pe.wait_ge(wqk_arrived, 32)
            for w in range(W_GROUPS):
                if w >= 2:
                    pe.wait_ge(proj_split, w - 1)
                if w == L:
                    pe.wait_ge(wc_arrived, 16 * L)
                for a in range(2):
                    for d in range(DT):
                        src = (wq_in, wk_in)[a][:, w, d * P:(d + 1) * P] if w < L else \
                            wc_in[:, w - L, a, d * P:(d + 1) * P]
                        at = (a * DT + d) * P if w < L else d * D + a * P
                        done = nc.tensor.transpose(bank(w)[:, at:at + P], src, ident[:, :])
                done.then_inc(proj_made, 1)
            for group in FIRST_ORDER[:AHEAD]:
                projection(0, 0, group)
            for g in FIRST:
                step(0, False, g)
            with pe.Fori(0, PAIRS - 1) as p:
                for g in BODY:
                    step(p, False, g)
            for g in BODY:
                step(PAIRS - 1, True, g)


_INS = ['x', 'adj', 'L0_gnn_Wq', 'L0_gnn_bq', 'L0_gnn_Wk', 'L0_gnn_bk', 'L0_gnn_Wc', 'L0_gnn_ln_g', 'L0_gnn_ln_b']


def kernel(**inputs):
    import numpy as _np
    import concourse.bacc as _bacc
    from concourse import mybir as _mybir
    from concourse.bass_utils import run_bass_kernel_spmd as _run

    nc = _bacc.Bacc("TRN2", target_bir_lowering=False, num_devices=1)
    arrays, args = {}, []
    for name in _INS:
        a = _np.ascontiguousarray(inputs[name])
        arrays[f"in_{name}"] = a
        args.append(nc.dram_tensor(f"in_{name}", a.shape, _mybir.dt.from_np(a.dtype), kind="ExternalInput").ap())
    args.append(nc.dram_tensor("out_0", inputs["x"].shape, _mybir.dt.float32, kind="ExternalOutput").ap())
    gnn_kernel(nc, *args)
    r = _run(nc, [arrays], core_ids=[0])
    return r.results[0]["out_0"]
```

```python
import concourse.bass as bass
from concourse import mybir
from contextlib import ExitStack


def gnn_kernel(nc, x, adj, wq, bq, wk, bk, wc, ln_g, ln_b, out):
    fp32 = mybir.dt.float32
    fp32r = mybir.dt.float32r
    bf16 = mybir.dt.bfloat16
    int32 = mybir.dt.int32
    ALU = mybir.AluOpType
    ACT = mybir.ActivationFunctionType

    P = 128
    NG, N, D = x.shape
    L, F, _ = wq.shape
    TILES = N // P
    DT = D // P
    PAIRS = NG // 2
    HALF = N // 2
    BANK = 512
    STAGES = 2 * L
    STEPS = STAGES * TILES
    EPS = 1e-5
    PENALTY = -1e30
    SCALE = float(F) ** 0.5
    NO_EDGE = -PENALTY / SCALE / 2

    SCHEDULE = [[("z", 2, 0), ("xT", 0, 1)], [("z", 3, 0), ("xT", 1, 1)], [("q", 0, 1)],
                [("k", 0, 1), ("xT", 2, 1)], [("z", 0, 1)], [("z", 1, 1), ("xT", 3, 1)], [("q", 1, 1)],
                [("k", 1, 1)]]
    AHEAD = [("wqk", 0), ("xT", 0), ("xT", 1), ("xT", 2), ("xT", 3), ("wc", 0), ("q", 0), ("k", 0), ("k", 1),
             ("q", 1)]
    BEHIND = [("z", 0), ("z", 1), ("wqk", 1), ("wc", 1)]
    FIRST_GROUPS = len(AHEAD + BEHIND)
    GROUPS = sum(map(len, SCHEDULE))
    ADJ_RING = 4
    RING = 4

    x_v = x.rearrange("g (j a p) d -> g j p a d", p=P, a=2)
    out_v = out.rearrange("g (j a p) d -> g j p a d", p=P, a=2)
    adj_v = adj.rearrange("g (t p) i -> g t p i", p=P)

    ctx = ExitStack()
    with ctx:
        def sb(name, shape, dt=fp32):
            return ctx.enter_context(nc.sbuf_tensor(name, shape, dt))

        def pb(name, shape):
            return ctx.enter_context(nc.psum_tensor(name, shape, fp32))

        def sem(name):
            return ctx.enter_context(nc.semaphore(name))

        def split(name, shape):
            return sb(name + "_high", shape, fp32r), sb(name + "_low", shape, fp32r)

        ident = sb("ident", [P, P])
        wq_in = sb("wq_in", [P, L, D])
        wk_in = sb("wk_in", [P, L, D])
        wc_in = sb("wc_in", [P, L, DT, D])
        bq_sb = sb("bq_sb", [P, L])
        bk_sb = sb("bk_sb", [P, L])
        gain = sb("gain", [P, L, D])
        shift = sb("shift", [P, L, D])
        minus_half = sb("minus_half", [P, 1])
        eps = sb("eps", [P, 1])
        wqk = [split(f"wqk{k}", [P, 2, DT * F]) for k in range(L)]
        wcT = [split(f"wcT{k}", [P, DT, D]) for k in range(L)]
        nodes = [sb(f"nodes{s}", [P, TILES, D]) for s in range(2)]
        penalty = [sb(f"penalty{s}", [P, TILES, N], bf16) for s in range(2)]
        adj_in = sb("adj_in", [P, ADJ_RING, N], int32)
        xT = split("xT", [P, DT, N])
        q = [split(f"q{s}", [P, N]) for s in range(2)]
        k = [split(f"k{s}", [P, N]) for s in range(2)]
        z = [sb(f"z{s}", [P, TILES, 2, D], fp32r) for s in range(2)]
        probs = [sb(f"probs{s}", [P, N]) for s in range(2)]
        pT = [split(f"pT{s}", [P, TILES, P]) for s in range(2)]
        neg_max = sb("neg_max", [P, RING])
        row_sum = sb("row_sum", [P, RING])
        inverse = sb("inverse", [P, RING])
        weight = sb("weight", [P, RING])
        part = sb("part", [P, D])
        y = sb("y", [P, RING, D])
        stats = sb("stats", [P, RING, 6])
        moments = sb("moments", [P, RING, 2])
        var_eps = sb("var_eps", [P, 1])
        rstd = sb("rstd", [P, 1])
        normed = sb("normed", [P, D])
        centred = sb("centred", [P, D])

        scores_ps = pb("scores_ps", [P, N])
        pT_ps = pb("pT_ps", [P, N])
        ctx_ps = [pb(f"ctx_ps{s}", [P, BANK]) for s in range(2)]
        proj_ps = [pb(f"proj_ps{s}", [P, BANK]) for s in range(2)]

        wqk_arrived = sem("wqk_arrived")
        wc_arrived = sem("wc_arrived")
        biases_in = sem("biases_in")
        vectors_in = sem("vectors_in")
        constants = sem("constants")
        x_in = [[sem(f"x_in{s}{j}") for j in range(TILES // 2)] for s in range(2)]
        stored = [[sem(f"stored{s}{j}") for j in range(TILES // 2)] for s in range(2)]
        adj_arrived = [sem(f"adj_arrived{r}") for r in range(ADJ_RING)]
        penalties = sem("penalties")
        proj_made = sem("proj_made")
        proj_high = sem("proj_high")
        proj_split = sem("proj_split")
        scores_made = sem("scores_made")
        masked = sem("masked")
        probs_made = sem("probs_made")
        pT_made = sem("pT_made")
        pT_high = sem("pT_high")
        pT_split = sem("pT_split")
        ctx_made = sem("ctx_made")
        inverted = sem("inverted")
        weighted = sem("weighted")
        part_made = sem("part_made")
        y_made = sem("y_made")
        stats_made = sem("stats_made")
        moments_made = sem("moments_made")
        norm_step = sem("norm_step")
        nodes_made = sem("nodes_made")

        block = ctx.enter_context(nc.Block())

        def dest(kind, j, s, part):
            if kind == "wqk":
                return wqk[j][part][:, :, :]
            if kind == "wc":
                return wcT[j][part][:, :, :]
            if kind == "xT":
                return xT[part][:, :, 2 * P * j:2 * P * (j + 1)]
            if kind == "z":
                return z[s % 2][:, 2 * j:2 * j + 2, part, :]
            return {"q": q, "k": k}[kind][s % 2][part][:, HALF * j:HALF * (j + 1)]

        def bank(n):
            return (proj_ps + ctx_ps)[n % 4] if n < len(AHEAD) else proj_ps[n % 2]

        def bank_free(n):
            return n - 3 if n < len(AHEAD) else n - 1

        def bank_as(n, kind):
            ps = bank(n)[:, :]
            return ps if kind in ("q", "k") else ps.rearrange("p (a c) -> p a c", a=2)

        PAIR_GROUPS = STAGES * GROUPS

        def stage_groups(last, s):
            return [(kind, j, s + on) for step in SCHEDULE for kind, j, on in step
                    if not (last and s + on >= STAGES)]

        def groups_of(last, g):
            s, t = g // TILES, g % TILES
            made = stage_groups(last, s)
            first = [(kind, j, 0, len(AHEAD) + i) for i, (kind, j) in enumerate(BEHIND)] if g == 0 else []
            return first + [(kind, j, s + on, FIRST_GROUPS + s * GROUPS + made.index((kind, j, s + on)))
                            for kind, j, on in SCHEDULE[t] if (kind, j, s + on) in made]

        AHEAD_GROUPS = [(kind, j, 0, i) for i, (kind, j) in enumerate(AHEAD)]

        def split_with(last, kind, j, s):
            if s == 0 and (kind, j) in AHEAD + BEHIND:
                return (AHEAD + BEHIND).index((kind, j)) + 1
            made_in = s if (kind, j, 0) in [group for step in SCHEDULE for group in step] else s - 1
            return FIRST_GROUPS + made_in * GROUPS + stage_groups(last, made_in).index((kind, j, s)) + 1

        FIRST = range(TILES)
        BODY = range(TILES, STEPS + TILES)

        def exists(p, last, u):
            return u >= 0 and not (last and u >= STEPS)

        @block.sync
        def _(sp):
            def load_adj(graph, t, r):
                sp.dma_start(adj_in[:, r, :], adj_v[graph, t]).then_inc(adj_arrived[r], 16)

            def load_x(graph, s, j):
                sp.dma_start(nodes[s][:, 2 * j:2 * j + 2, :], x_v[graph, j]).then_inc(x_in[s][j], 16)

            def step(p, last, g):
                s, t = g // TILES, g % TILES
                for side in range(2):
                    j, odd = divmod(g - TILES * (2 + side) - 5, 2)
                    if odd == 0 and 0 <= j < TILES // 2:
                        sp.wait_ge(nodes_made, p * STEPS + (TILES * (2 + side) + 2 * j + 2))
                        sp.dma_start(out_v[p * 2 + side, j],
                                     nodes[side][:, 2 * j:2 * j + 2, :]).then_inc(stored[side][j], 16)
                    if odd == 1 and 0 <= j < TILES // 2 and not last:
                        sp.wait_ge(stored[side][j], p * 16 + 16)
                        load_x(p * 2 + (2 + side), side, j)
                if s == 4 and not last and t < ADJ_RING:
                    sp.wait_ge(penalties, p * 16 + (24 + t + 1))
                    load_adj(p * 2 + 3, ADJ_RING + t, t)
                if s == 1 and not last and t < ADJ_RING:
                    sp.wait_ge(penalties, p * 16 + (12 + t + 1))
                    load_adj(p * 2 + 2, t, t)
                if s == 3 and not last:
                    sp.wait_ge(penalties, p * 16 + (16 + t + 1))
                    load_adj(p * 2 + (2 if t < ADJ_RING else 3), (ADJ_RING + t) % TILES, t % ADJ_RING)

            for w_in, w in ((wq_in, wq), (wk_in, wk)):
                sp.dma_start(w_in[:, :, :], w.rearrange("l f d -> f l d")).then_inc(wqk_arrived, 16)
            for j in range(TILES // 2):
                load_x(0, 0, j)
            for layer in range(L):
                sp.dma_start(wc_in[:, layer], wc[layer].rearrange("(a p) d -> p a d", p=P)).then_inc(wc_arrived, 16)
            for t in range(ADJ_RING):
                load_adj(0, t, t)
            for j in range(TILES // 2):
                load_x(1, 1, j)
            for n in range(2 * TILES - ADJ_RING):
                sp.wait_ge(penalties, n + 1)
                load_adj((ADJ_RING + n) // TILES, (ADJ_RING + n) % TILES, n % ADJ_RING)
            for g in FIRST:
                step(0, False, g)
            with sp.Fori(0, PAIRS - 1) as p:
                for g in BODY:
                    step(p, False, g)
            for g in BODY:
                step(PAIRS - 1, True, g)
            for side in range(2):
                for j in range(TILES // 2):
                    sp.wait_ge(stored[side][j], 16 * PAIRS)

        @block.gpsimd
        def _(pool):
            nc.gpsimd.memset(ident[:, :], 0.0).then_inc(constants, 1)
            pool.wait_ge(constants, 1)
            nc.gpsimd.affine_select(out=ident[:, :], in_=ident[:, :], compare_op=ALU.not_equal, fill=1.0,
                                    base=0, pattern=[[-1, P]], channel_multiplier=1).then_inc(constants, 1)
            nc.gpsimd.memset(minus_half[:, :], -0.5).then_inc(constants, 1)
            nc.gpsimd.memset(eps[:, :], EPS).then_inc(constants, 1)
            with nc.allow_non_contiguous_dma(reason="a few bias values, once"):
                for b_sb, b in ((bq_sb, bq), (bk_sb, bk)):
                    pool.dma_start(b_sb[:, :], b.rearrange("l f -> f l")).then_inc(biases_in, 16)
            for v_sb, v in ((gain, ln_g), (shift, ln_b)):
                pool.dma_start(v_sb[:, :, :], v[None, :, :].to_broadcast([P, L, D])).then_inc(vectors_in, 16)

            pool.wait_ge(vectors_in, 32)
            pool.wait_ge(constants, 4)

            with pool.Fori(0, PAIRS) as p:
                for u in range(STEPS):
                    s, t = u // TILES, u % TILES
                    layer, r = s // 2, u % RING
                    done = p * (STEPS * 5) + 5 * u
                    pool.wait_ge(moments_made, p * STEPS + (u + 1))
                    nc.gpsimd.tensor_tensor(var_eps[:, :], moments[:, r, 1:2], eps[:, :],
                                            ALU.add).then_inc(norm_step, 1)
                    pool.wait_ge(norm_step, done + 1)
                    nc.gpsimd.tensor_tensor(rstd[:, :], var_eps[:, :], minus_half[:, :],
                                            ALU.pow).then_inc(norm_step, 1)
                    nc.gpsimd.tensor_tensor(centred[:, :], y[:, r, :], moments[:, r, 0:1].to_broadcast([P, D]),
                                            ALU.subtract).then_inc(norm_step, 1)
                    pool.wait_ge(norm_step, done + 3)
                    nc.gpsimd.tensor_tensor(normed[:, :], centred[:, :], rstd[:, :].to_broadcast([P, D]),
                                            ALU.mult).then_inc(norm_step, 1)
                    pool.wait_ge(norm_step, done + 4)
                    nc.gpsimd.tensor_tensor(centred[:, :], normed[:, :], gain[:, layer, :],
                                            ALU.mult).then_inc(norm_step, 1)
                    pool.wait_ge(norm_step, done + 5)
                    nc.gpsimd.tensor_tensor(nodes[s % 2][:, t, :], centred[:, :], shift[:, layer, :],
                                            ALU.add).then_inc(nodes_made, 1)

        @block.scalar
        def _(act):
            def projections(p, groups):
                for kind, j, s, n in groups:
                    act.wait_ge(proj_made, p * PAIR_GROUPS + (n + 1))
                    bias = {"q": bq_sb, "k": bk_sb}.get(kind)
                    layer = s // 2 % L
                    nc.scalar.activation(dest(kind, j, s, 0), bank_as(n, kind), ACT.Identity,
                                         bias=0.0 if bias is None else bias[:, layer:layer + 1],
                                         ).then_inc(proj_high, 1)

            def step(p, last, g):
                s, t = g // TILES, g % TILES
                u = g - 2
                if exists(p, last, u):
                    for h in range(2):
                        act.wait_ge(pT_made, p * (2 * STEPS) + (2 * u + h + 1))
                        nc.scalar.activation(pT[u % 2][0][:, 4 * h:4 * h + 4, :],
                                             pT_ps[:, BANK * h:BANK * (h + 1)].rearrange("p (a c) -> p a c", c=P),
                                             ACT.Identity).then_inc(pT_high, 1)
                if exists(p, last, g):
                    r = g % RING
                    act.wait_ge(masked, p * STEPS + (g + 1))
                    nc.scalar.activation(probs[g % 2][:, :], probs[g % 2][:, :], ACT.Exp,
                                         bias=neg_max[:, r:r + 1], scale=-1.0,
                                         accum_out=row_sum[:, r:r + 1]).then_inc(probs_made, 1)
                projections(p, groups_of(last, g))

            act.wait_ge(biases_in, 32)
            projections(0, AHEAD_GROUPS)
            for g in FIRST:
                step(0, False, g)
            with act.Fori(0, PAIRS - 1) as p:
                for g in BODY:
                    step(p, False, g)
            for g in BODY:
                step(PAIRS - 1, True, g)

        @block.vector
        def _(dve):
            def projections(p, groups):
                for kind, j, s, n in groups:
                    dve.wait_ge(proj_high, p * PAIR_GROUPS + (n + 1))
                    high, low = dest(kind, j, s, 0).bitcast(fp32), dest(kind, j, s, 1)
                    if kind in ("q", "k"):
                        bias, layer = {"q": bq_sb, "k": bk_sb}[kind], s // 2 % L
                        nc.vector.scalar_tensor_tensor(out=low, in0=bank_as(n, kind), scalar=bias[:, layer:layer + 1],
                                                       in1=high, op0=ALU.add, op1=ALU.subtract).then_inc(proj_split, 1)
                    else:
                        nc.vector.tensor_tensor(low, bank_as(n, kind), high, ALU.subtract).then_inc(proj_split, 1)

            def make_penalty(p, n):
                r = n % ADJ_RING
                dve.wait_ge(adj_arrived[r], p * 64 + 16 * (n // ADJ_RING + 1))
                nc.vector.tensor_scalar(penalty[n // TILES % 2][:, n % TILES, :], adj_in[:, r, :], 0.0, PENALTY,
                                        ALU.is_equal, ALU.mult).then_inc(penalties, 1)

            def step(p, last, g):
                s, t = g // TILES, g % TILES
                u = g - 3
                if exists(p, last, u):
                    r = u % RING
                    dve.wait_ge(ctx_made, p * STEPS + (u + 1))
                    dve.wait_ge(weighted, p * STEPS + (u + 1))
                    if u >= RING:
                        dve.wait_ge(nodes_made, p * STEPS + (u - RING + 1))
                    nc.vector.scalar_tensor_tensor(out=part[:, :], in0=ctx_ps[u % 2][:, D:2 * D],
                                                   scalar=weight[:, r:r + 1],
                                                   in1=nodes[u // TILES % 2][:, u % TILES, :],
                                                   op0=ALU.mult, op1=ALU.add).then_inc(part_made, 1)
                v = g - 2
                if exists(p, last, v):
                    for h in range(2):
                        dve.wait_ge(pT_high, p * (2 * STEPS) + (2 * v + h + 1))
                        nc.vector.tensor_tensor(pT[v % 2][1][:, 4 * h:4 * h + 4, :],
                                                pT_ps[:, BANK * h:BANK * (h + 1)].rearrange("p (a c) -> p a c", c=P),
                                                pT[v % 2][0][:, 4 * h:4 * h + 4, :].bitcast(fp32),
                                                ALU.subtract).then_inc(pT_split, 1)
                if exists(p, last, u):
                    r = u % RING
                    dve.wait_ge(part_made, p * STEPS + (u + 1))
                    nc.vector.scalar_tensor_tensor(out=y[:, r, :], in0=ctx_ps[u % 2][:, 0:D],
                                                   scalar=weight[:, r:r + 1], in1=part[:, :],
                                                   op0=ALU.mult, op1=ALU.add).then_inc(y_made, 1)
                if exists(p, last, g):
                    if s == 0:
                        dve.wait_ge(penalties, t + 1)
                    elif t == 0 and s % STAGES < 2:
                        dve.wait_ge(penalties, p * 16 + (16 * (s // STAGES) + 8 * (s % STAGES + 1)))
                    dve.wait_ge(scores_made, p * STEPS + (g + 1))
                if exists(p, last, v):
                    r = v % RING
                    nc.vector.reciprocal(inverse[:, r:r + 1], row_sum[:, r:r + 1]).then_inc(inverted, 1)
                if exists(p, last, g):
                    r = g % RING
                    nc.vector.tensor_tensor_reduce(out=probs[g % 2][:, :], in0=scores_ps[:, :],
                                                   in1=penalty[s % 2][:, t, :], scale=-1.0 / SCALE, scalar=3e38,
                                                   op0=ALU.add, op1=ALU.min,
                                                   accum_out=neg_max[:, r:r + 1]).then_inc(masked, 1)
                if exists(p, last, v):
                    r = v % RING
                    dve.wait_ge(inverted, p * STEPS + (v + 1))
                    nc.vector.tensor_scalar(weight[:, r:r + 1], neg_max[:, r:r + 1], NO_EDGE,
                                            inverse[:, r:r + 1], ALU.is_lt, ALU.mult).then_inc(weighted, 1)
                if exists(p, last, u):
                    r = u % RING
                    dve.wait_ge(y_made, p * STEPS + (u + 1))
                    nc.vector.bn_stats(stats[:, r, :], y[:, r, :]).then_inc(stats_made, 1)
                if s == 0:
                    for n in range(2 + 2 * t, min(4 + 2 * t, 2 * TILES)):
                        make_penalty(p, n)
                if s in (3, 4) and not last:
                    make_penalty(p, 2 * TILES + TILES * (s - 3) + t)
                if exists(p, last, u):
                    dve.wait_ge(stats_made, p * STEPS + (u + 1))
                groups = groups_of(last, g)
                projections(p, groups[:1])
                if exists(p, last, u):
                    r = u % RING
                    nc.vector.bn_aggr(moments[:, r, :], stats[:, r, :]).then_inc(moments_made, 1)
                projections(p, groups[1:])

            dve.wait_ge(biases_in, 32)
            projections(0, AHEAD_GROUPS)
            for t in range(2):
                make_penalty(0, t)
            for g in FIRST:
                step(0, False, g)
            with dve.Fori(0, PAIRS - 1) as p:
                for g in BODY:
                    step(p, False, g)
            for g in BODY:
                step(PAIRS - 1, True, g)

        @block.tensor
        def _(pe):
            def product(ps, terms):
                for i, (a, b) in enumerate(terms):
                    last = nc.tensor.matmul(ps, a, b, start=i == 0, stop=i == len(terms) - 1)
                return last

            def three(high_low_a, high_low_b):
                (ah, al), (bh, bl) = high_low_a, high_low_b
                return [(ah, bh), (ah, bl), (al, bh)]

            def projection(p, last, kind, j, s, n):
                layer, side = s // 2 % L, s % 2
                free = bank_free(n)
                if kind in ("q", "k"):
                    free = max(free, split_with(last, "xT", 2 * j + 1, s))
                if kind == "z":
                    free = max(free, split_with(last, "xT", j, s))
                if s == 0 and kind in ("q", "z"):
                    free = max(free, split_with(last, "wqk" if kind == "q" else "wc", 0, 0))
                if free > 0:
                    pe.wait_ge(proj_split, p * PAIR_GROUPS + free)
                if kind in ("wqk", "wc"):
                    if kind == "wqk":
                        pe.wait_ge(wqk_arrived, 32)
                    else:
                        pe.wait_ge(wc_arrived, 16 * L)
                    for a in range(2):
                        for d in range(DT):
                            src = (wq_in, wk_in)[a][:, j, d * P:(d + 1) * P] if kind == "wqk" else \
                                wc_in[:, j, a, d * P:(d + 1) * P]
                            at = (a * DT + d) * P if kind == "wqk" else d * D + a * P
                            done = nc.tensor.transpose(bank(n)[:, at:at + P], src, ident[:, :])
                elif kind == "xT":
                    if layer == 0:
                        pe.wait_ge(x_in[side][j], p * 16 + 16 * (s // STAGES + 1))
                    else:
                        pe.wait_ge(nodes_made, p * STEPS + (TILES * (s - 2) + 2 * j + 2))
                    for a in range(2):
                        for d in range(DT):
                            done = nc.tensor.transpose(bank_as(n, kind)[:, d, a * P:(a + 1) * P],
                                                       nodes[side][:, 2 * j + a, d * P:(d + 1) * P], ident[:, :])
                elif kind == "z":
                    high_low_w = wcT[layer]
                    for a in range(2):
                        c = (2 * j + a) * P
                        done = product(bank(n)[:, a * D:(a + 1) * D],
                                       [pair for d in range(DT)
                                        for pair in three([part[:, d, c:c + P] for part in xT],
                                                          [part[:, d, :] for part in high_low_w])])
                else:
                    m = 0 if kind == "q" else 1
                    done = product(bank(n)[:, :],
                                   [pair for d in range(DT)
                                    for pair in three([part[:, m, d * F:(d + 1) * F] for part in wqk[layer]],
                                                      [part[:, d, HALF * j:HALF * (j + 1)] for part in xT])])
                done.then_inc(proj_made, 1)

            def step(p, last, g):
                s, t = g // TILES, g % TILES
                side = s % 2
                if exists(p, last, g):
                    if t == 0:
                        pe.wait_ge(proj_split, p * PAIR_GROUPS + max(split_with(last, kind, 1, s)
                                                                     for kind in ("q", "k")))
                    if g > 0:
                        pe.wait_ge(masked, p * STEPS + g)
                    rows = slice(t * P, (t + 1) * P)
                    (qh, ql), (kh, kl) = q[side], k[side]
                    halves = [(scores_ps[:, HALF * h:HALF * (h + 1)], slice(HALF * h, HALF * (h + 1)))
                              for h in range(2)]
                    for ps, cols in halves:
                        nc.tensor.matmul(ps, qh[:, rows], kh[:, cols], start=True, stop=False)
                        nc.tensor.matmul(ps, qh[:, rows], kl[:, cols], start=False, stop=False)
                    for ps, cols in halves:
                        done = nc.tensor.matmul(ps, ql[:, rows], kh[:, cols], start=False, stop=True)
                    done.then_inc(scores_made, 1)
                for group in groups_of(last, g):
                    projection(p, last, *group)
                v = g - 1
                if exists(p, last, v):
                    pe.wait_ge(probs_made, p * STEPS + (v + 1))
                    for i in range(TILES):
                        if i % 4 == 0 and v > 0:
                            pe.wait_ge(pT_split, p * (2 * STEPS) + (2 * (v - 1) + i // 4 + 1))
                        done = nc.tensor.transpose(pT_ps[:, i * P:(i + 1) * P],
                                                   probs[v % 2][:, i * P:(i + 1) * P], ident[:, :])
                        if i % 4 == 3:
                            done.then_inc(pT_made, 1)
                u = g - 2
                if exists(p, last, u):
                    if u % TILES == 0:
                        pe.wait_ge(proj_split, p * PAIR_GROUPS + split_with(last, "z", 3, u // TILES))
                    zz, ps = z[u // TILES % 2], ctx_ps[u % 2]
                    pe.wait_ge(pT_split, p * (2 * STEPS) + (2 * u + 2))
                    (high, low) = pT[u % 2]
                    for i in range(TILES):
                        nc.tensor.matmul(ps[:, :], high[:, i, :], zz[:, i, :, :].rearrange("p a d -> p (a d)"),
                                         start=i == 0, stop=False)
                        done = nc.tensor.matmul(ps[:, 0:D], low[:, i, :], zz[:, i, 0, :],
                                                start=False, stop=i == TILES - 1)
                    done.then_inc(ctx_made, 1)

            pe.wait_ge(constants, 2)
            for group in AHEAD_GROUPS:
                projection(0, False, *group)
            for g in FIRST:
                step(0, False, g)
            with pe.Fori(0, PAIRS - 1) as p:
                for g in BODY:
                    step(p, False, g)
            for g in BODY:
                step(PAIRS - 1, True, g)


_INS = ['x', 'adj', 'L0_gnn_Wq', 'L0_gnn_bq', 'L0_gnn_Wk', 'L0_gnn_bk', 'L0_gnn_Wc', 'L0_gnn_ln_g', 'L0_gnn_ln_b']


def kernel(**inputs):
    import numpy as _np
    import concourse.bacc as _bacc
    from concourse import mybir as _mybir
    from concourse.bass_utils import run_bass_kernel_spmd as _run

    nc = _bacc.Bacc("TRN2", target_bir_lowering=False, num_devices=1)
    arrays, args = {}, []
    for name in _INS:
        a = _np.ascontiguousarray(inputs[name])
        arrays[f"in_{name}"] = a
        args.append(nc.dram_tensor(f"in_{name}", a.shape, _mybir.dt.from_np(a.dtype), kind="ExternalInput").ap())
    args.append(nc.dram_tensor("out_0", inputs["x"].shape, _mybir.dt.float32, kind="ExternalOutput").ap())
    gnn_kernel(nc, *args)
    r = _run(nc, [arrays], core_ids=[0])
    return r.results[0]["out_0"]
```

```python
import concourse.bass as bass
from concourse import mybir
from contextlib import ExitStack


def gnn_kernel(nc, x, adj, wq, bq, wk, bk, wc, ln_g, ln_b, out):
    fp32 = mybir.dt.float32
    fp32r = mybir.dt.float32r
    bf16 = mybir.dt.bfloat16
    int32 = mybir.dt.int32
    ALU = mybir.AluOpType
    ACT = mybir.ActivationFunctionType

    P = 128
    NG, N, D = x.shape
    L, F, _ = wq.shape
    TILES = N // P
    DT = D // P
    PAIRS = NG // 2
    HALF = N // 2
    BANK = 512
    STAGES = 2 * L
    STEPS = STAGES * TILES
    EPS = 1e-5
    PENALTY = -1e30
    SCALE = float(F) ** 0.5
    NO_EDGE = -PENALTY / SCALE / 2

    SCHEDULE = [[("z", 2, 0), ("xT", 0, 1)], [("z", 3, 0), ("xT", 1, 1)], [("q", 0, 1)],
                [("k", 0, 1), ("xT", 2, 1)], [("z", 0, 1)], [("z", 1, 1), ("xT", 3, 1)], [("q", 1, 1)],
                [("k", 1, 1)]]
    AHEAD = [("wqk", 0), ("xT", 0), ("xT", 1), ("xT", 2), ("xT", 3), ("q", 0), ("k", 0), ("k", 1), ("wc", 0),
             ("q", 1)]
    FIRST_Q = AHEAD.index(("q", 0))
    BEHIND = [("z", 0), ("z", 1), ("wqk", 1), ("wc", 1)]
    FIRST_GROUPS = len(AHEAD + BEHIND)
    WIDE = FIRST_GROUPS + len(SCHEDULE[0])
    GROUPS = sum(map(len, SCHEDULE))
    WARM_UP = 7
    ADJ_RING = 4
    RING = 4

    x_v = x.rearrange("g (j a p) d -> g j p a d", p=P, a=2)
    out_v = out.rearrange("g (j a p) d -> g j p a d", p=P, a=2)
    adj_v = adj.rearrange("g (t p) i -> g t p i", p=P)

    ctx = ExitStack()
    with ctx:
        def sb(name, shape, dt=fp32):
            return ctx.enter_context(nc.sbuf_tensor(name, shape, dt))

        def pb(name, shape):
            return ctx.enter_context(nc.psum_tensor(name, shape, fp32))

        def sem(name):
            return ctx.enter_context(nc.semaphore(name))

        def split(name, shape):
            return sb(name + "_high", shape, fp32r), sb(name + "_low", shape, fp32r)

        ident = sb("ident", [P, P])
        wq_in = sb("wq_in", [P, L, D])
        wk_in = sb("wk_in", [P, L, D])
        wc_in = sb("wc_in", [P, L, DT, D])
        bq_sb = sb("bq_sb", [P, L])
        bk_sb = sb("bk_sb", [P, L])
        gain = sb("gain", [P, L, D])
        shift = sb("shift", [P, L, D])
        minus_half = sb("minus_half", [P, 1])
        eps = sb("eps", [P, 1])
        table_loaded = sb("table_loaded", [P, 1])
        wqk = [split(f"wqk{k}", [P, 2, DT * F]) for k in range(L)]
        wcT = [split(f"wcT{k}", [P, DT, D]) for k in range(L)]
        nodes = [sb(f"nodes{s}", [P, TILES, D]) for s in range(2)]
        penalty = [sb(f"penalty{s}", [P, TILES, N], bf16) for s in range(2)]
        adj_in = sb("adj_in", [P, ADJ_RING, N], int32)
        xT = split("xT", [P, DT, N])
        q = [split(f"q{s}", [P, N]) for s in range(2)]
        k = [split(f"k{s}", [P, N]) for s in range(2)]
        z = [sb(f"z{s}", [P, TILES, 2, D], fp32r) for s in range(2)]
        probs = [sb(f"probs{s}", [P, N]) for s in range(2)]
        pT = [split(f"pT{s}", [P, TILES, P]) for s in range(2)]
        neg_max = sb("neg_max", [P, RING])
        row_sum = sb("row_sum", [P, RING])
        inverse = sb("inverse", [P, RING])
        weight = sb("weight", [P, RING])
        part = sb("part", [P, D])
        y = sb("y", [P, RING, D])
        stats = sb("stats", [P, RING, 6])
        moments = sb("moments", [P, RING, 2])
        var_eps = sb("var_eps", [P, 1])
        rstd = sb("rstd", [P, 1])
        last_var_eps = sb("last_var_eps", [P, 2])
        last_rstd = sb("last_rstd", [P, 2])
        normed = sb("normed", [P, D])
        centred = sb("centred", [P, D])

        scores_ps = pb("scores_ps", [P, N])
        pT_ps = pb("pT_ps", [P, N])
        ctx_ps = [pb(f"ctx_ps{s}", [P, BANK]) for s in range(2)]
        proj_ps = [pb(f"proj_ps{s}", [P, BANK]) for s in range(2)]

        wqk_arrived = [sem(f"wqk_arrived{k}") for k in range(L)]
        wc_arrived = sem("wc_arrived")
        biases_in = sem("biases_in")
        vectors_in = sem("vectors_in")
        constants = sem("constants")
        x_in = [[sem(f"x_in{s}{j}") for j in range(TILES // 2)] for s in range(2)]
        stored = [[sem(f"stored{s}{j}") for j in range(TILES // 2)] for s in range(2)]
        adj_arrived = [sem(f"adj_arrived{r}") for r in range(ADJ_RING)]
        penalties = sem("penalties")
        early_penalties = sem("early_penalties")
        proj_made = sem("proj_made")
        proj_high = sem("proj_high")
        proj_split = sem("proj_split")
        scores_made = sem("scores_made")
        masked = sem("masked")
        probs_made = sem("probs_made")
        pT_made = sem("pT_made")
        pT_high = sem("pT_high")
        pT_split = sem("pT_split")
        ctx_made = sem("ctx_made")
        inverted = sem("inverted")
        weighted = sem("weighted")
        part_made = sem("part_made")
        y_made = sem("y_made")
        stats_made = sem("stats_made")
        moments_made = sem("moments_made")
        norm_step = sem("norm_step")
        last_var_made = sem("last_var_made")
        last_rstd_made = sem("last_rstd_made")
        last_norm_step = sem("last_norm_step")
        last_tiles_made = sem("last_tiles_made")
        nodes_made = sem("nodes_made")

        block = ctx.enter_context(nc.Block())

        def dest(kind, j, s, part):
            if kind == "wqk":
                return wqk[j][part][:, :, :]
            if kind == "wc":
                return wcT[j][part][:, :, :]
            if kind == "xT":
                return xT[part][:, :, 2 * P * j:2 * P * (j + 1)]
            if kind == "z":
                return z[s % 2][:, 2 * j:2 * j + 2, part, :]
            return {"q": q, "k": k}[kind][s % 2][part][:, HALF * j:HALF * (j + 1)]

        EARLY = TILES

        def make_penalty(engine, wait_ge, p, n, made):
            r = n % ADJ_RING
            wait_ge(adj_arrived[r], p * 64 + 16 * (n // ADJ_RING + 1))
            engine.tensor_scalar(penalty[n // TILES % 2][:, n % TILES, :], adj_in[:, r, :], 0.0, PENALTY,
                                 ALU.is_equal, ALU.mult).then_inc(made, 1)

        def bank(n):
            return (proj_ps + ctx_ps)[n % 4] if n < WIDE else proj_ps[n % 2]

        def bank_free(n):
            return n - 3 if n < WIDE else n - 1

        def bank_as(n, kind):
            ps = bank(n)[:, :]
            return ps if kind in ("q", "k") else ps.rearrange("p (a c) -> p a c", a=2)

        PAIR_GROUPS = STAGES * GROUPS

        def stage_groups(last, s):
            return [(kind, j, s + on) for step in SCHEDULE for kind, j, on in step
                    if not (last and s + on >= STAGES)]

        def groups_of(last, g):
            s, t = g // TILES, g % TILES
            made = stage_groups(last, s)
            first = [(kind, j, 0, len(AHEAD) + i) for i, (kind, j) in enumerate(BEHIND)] if g == 0 else []
            return first + [(kind, j, s + on, FIRST_GROUPS + s * GROUPS + made.index((kind, j, s + on)))
                            for kind, j, on in SCHEDULE[t] if (kind, j, s + on) in made]

        AHEAD_GROUPS = [(kind, j, 0, i) for i, (kind, j) in enumerate(AHEAD)]

        def split_with(last, kind, j, s):
            if s == 0 and (kind, j) in AHEAD + BEHIND:
                return (AHEAD + BEHIND).index((kind, j)) + 1
            made_in = s if (kind, j, 0) in [group for step in SCHEDULE for group in step] else s - 1
            return FIRST_GROUPS + made_in * GROUPS + stage_groups(last, made_in).index((kind, j, s)) + 1

        FIRST = range(TILES)
        BODY = range(TILES, STEPS + TILES)

        def exists(p, last, u):
            return u >= 0 and not (last and u >= STEPS)

        @block.sync
        def _(sp):
            def load_adj(graph, t, r):
                sp.dma_start(adj_in[:, r, :], adj_v[graph, t]).then_inc(adj_arrived[r], 16)

            def load_x(graph, s, j):
                sp.dma_start(nodes[s][:, 2 * j:2 * j + 2, :], x_v[graph, j]).then_inc(x_in[s][j], 16)

            def step(p, last, g):
                s, t = g // TILES, g % TILES
                for side in range(2):
                    j, odd = divmod(g - TILES * (2 + side) - 5, 2)
                    if odd == 0 and 0 <= j < TILES // 2:
                        if last and side == 1 and j == TILES // 2 - 1:
                            sp.wait_ge(last_tiles_made, 2)
                        else:
                            sp.wait_ge(nodes_made, p * STEPS + (TILES * (2 + side) + 2 * j + 2))
                        sp.dma_start(out_v[p * 2 + side, j],
                                     nodes[side][:, 2 * j:2 * j + 2, :]).then_inc(stored[side][j], 16)
                    if odd == 1 and 0 <= j < TILES // 2 and not last:
                        sp.wait_ge(stored[side][j], p * 16 + 16)
                        load_x(p * 2 + (2 + side), side, j)
                if s == 4 and not last and t < ADJ_RING:
                    sp.wait_ge(penalties, p * 16 + (24 + t + 1 - EARLY))
                    load_adj(p * 2 + 3, ADJ_RING + t, t)
                if s == 1 and not last and t < ADJ_RING:
                    sp.wait_ge(penalties, p * 16 + (16 - EARLY))
                    sp.wait_ge(early_penalties, EARLY)
                    load_adj(p * 2 + 2, t, t)
                if s == 3 and not last:
                    sp.wait_ge(penalties, p * 16 + (16 + t + 1 - EARLY))
                    load_adj(p * 2 + (2 if t < ADJ_RING else 3), (ADJ_RING + t) % TILES, t % ADJ_RING)

            def load_wqk(layer):
                for w_in, w in ((wq_in, wq), (wk_in, wk)):
                    sp.dma_start(w_in[:, layer, :], w[layer]).then_inc(wqk_arrived[layer], 16)

            load_wqk(0)
            for j in range(TILES // 2):
                load_x(0, 0, j)
            for layer in range(L):
                sp.dma_start(wc_in[:, layer], wc[layer].rearrange("(a p) d -> p a d", p=P)).then_inc(wc_arrived, 16)
            for t in range(ADJ_RING):
                load_adj(0, t, t)
            for layer in range(1, L):
                load_wqk(layer)
            for j in range(TILES // 2):
                load_x(1, 1, j)
            for n in range(2 * TILES - ADJ_RING):
                sp.wait_ge((early_penalties, penalties)[n % 2], n // 2 + 1)
                load_adj((ADJ_RING + n) // TILES, (ADJ_RING + n) % TILES, n % ADJ_RING)
            for g in FIRST:
                step(0, False, g)
            with sp.Fori(0, PAIRS - 1) as p:
                for g in BODY:
                    step(p, False, g)
            for g in BODY:
                step(PAIRS - 1, True, g)
            for side in range(2):
                for j in range(TILES // 2):
                    sp.wait_ge(stored[side][j], 16 * PAIRS)

        @block.gpsimd
        def _(pool):
            nc.gpsimd.memset(ident[:, :], 0.0).then_inc(constants, 1)
            pool.wait_ge(constants, 1)
            nc.gpsimd.affine_select(out=ident[:, :], in_=ident[:, :], compare_op=ALU.not_equal, fill=1.0,
                                    base=0, pattern=[[-1, P]], channel_multiplier=1).then_inc(constants, 1)
            nc.gpsimd.memset(minus_half[:, :], -0.5).then_inc(constants, 1)
            nc.gpsimd.memset(eps[:, :], EPS).then_inc(constants, 1)
            with nc.allow_non_contiguous_dma(reason="a few bias values, once"):
                for b_sb, b in ((bq_sb, bq), (bk_sb, bk)):
                    pool.dma_start(b_sb[:, :], b.rearrange("l f -> f l")).then_inc(biases_in, 16)
            for v_sb, v in ((gain, ln_g), (shift, ln_b)):
                pool.dma_start(v_sb[:, :, :], v[None, :, :].to_broadcast([P, L, D])).then_inc(vectors_in, 16)

            for n in range(0, 2 * TILES, 2):
                make_penalty(nc.gpsimd, pool.wait_ge, 0, n, early_penalties)

            pool.wait_ge(vectors_in, 32)
            pool.wait_ge(constants, 4)

            def norm(p, u):
                s, t = u // TILES, u % TILES
                layer, r = s // 2, u % RING
                done = p * (STEPS * 5) + 5 * u
                pool.wait_ge(moments_made, p * STEPS + (u + 1))
                nc.gpsimd.tensor_tensor(var_eps[:, :], moments[:, r, 1:2], eps[:, :],
                                        ALU.add).then_inc(norm_step, 1)
                pool.wait_ge(norm_step, done + 1)
                nc.gpsimd.tensor_tensor(rstd[:, :], var_eps[:, :], minus_half[:, :],
                                        ALU.pow).then_inc(norm_step, 1)
                nc.gpsimd.tensor_tensor(centred[:, :], y[:, r, :], moments[:, r, 0:1].to_broadcast([P, D]),
                                        ALU.subtract).then_inc(norm_step, 1)
                pool.wait_ge(norm_step, done + 3)
                nc.gpsimd.tensor_tensor(normed[:, :], centred[:, :], rstd[:, :].to_broadcast([P, D]),
                                        ALU.mult).then_inc(norm_step, 1)
                pool.wait_ge(norm_step, done + 4)
                nc.gpsimd.tensor_tensor(centred[:, :], normed[:, :], gain[:, layer, :],
                                        ALU.mult).then_inc(norm_step, 1)
                pool.wait_ge(norm_step, done + 5)
                nc.gpsimd.tensor_tensor(nodes[s % 2][:, t, :], centred[:, :], shift[:, layer, :],
                                        ALU.add).then_inc(nodes_made, 1)

            with pool.Fori(0, PAIRS - 1) as p:
                for u in range(STEPS):
                    norm(p, u)
            for u in range(STEPS - 2):
                norm(PAIRS - 1, u)
            for i in range(2):
                u = STEPS - 2 + i
                pool.wait_ge(moments_made, (PAIRS - 1) * STEPS + u + 1)
                nc.gpsimd.tensor_tensor(last_var_eps[:, i:i + 1], moments[:, u % RING, 1:2], eps[:, :],
                                        ALU.add).then_inc(last_var_made, 1)
                pool.wait_ge(last_var_made, i + 1)
                nc.gpsimd.tensor_tensor(last_rstd[:, i:i + 1], last_var_eps[:, i:i + 1], minus_half[:, :],
                                        ALU.pow).then_inc(last_rstd_made, 1)

        @block.scalar
        def _(act):
            act.wait_ge(constants, 2)
            nc.scalar.activation(table_loaded[:, :], ident[:, 0:1], ACT.Exp)

            def projections(p, groups):
                for kind, j, s, n in groups:
                    act.wait_ge(proj_made, p * PAIR_GROUPS + (n + 1))
                    bias = {"q": bq_sb, "k": bk_sb}.get(kind)
                    layer = s // 2 % L
                    nc.scalar.activation(dest(kind, j, s, 0), bank_as(n, kind), ACT.Identity,
                                         bias=0.0 if bias is None else bias[:, layer:layer + 1],
                                         ).then_inc(proj_high, 1)

            def step(p, last, g):
                s, t = g // TILES, g % TILES
                u = g - 2
                if exists(p, last, u):
                    for h in range(2):
                        act.wait_ge(pT_made, p * (2 * STEPS) + (2 * u + h + 1))
                        nc.scalar.activation(pT[u % 2][0][:, 4 * h:4 * h + 4, :],
                                             pT_ps[:, BANK * h:BANK * (h + 1)].rearrange("p (a c) -> p a c", c=P),
                                             ACT.Identity).then_inc(pT_high, 1)
                if exists(p, last, g):
                    r = g % RING
                    act.wait_ge(masked, p * STEPS + (g + 1))
                    nc.scalar.activation(probs[g % 2][:, :], probs[g % 2][:, :], ACT.Exp,
                                         bias=neg_max[:, r:r + 1], scale=-1.0,
                                         accum_out=row_sum[:, r:r + 1]).then_inc(probs_made, 1)
                projections(p, groups_of(last, g))

            projections(0, AHEAD_GROUPS[:FIRST_Q])
            act.wait_ge(biases_in, 32)
            projections(0, AHEAD_GROUPS[FIRST_Q:])
            for g in FIRST:
                step(0, False, g)
            with act.Fori(0, PAIRS - 1) as p:
                for g in BODY:
                    step(p, False, g)
            for g in BODY:
                step(PAIRS - 1, True, g)

        @block.vector
        def _(dve):
            def projections(p, groups):
                for kind, j, s, n in groups:
                    dve.wait_ge(proj_high, p * PAIR_GROUPS + (n + 1))
                    high, low = dest(kind, j, s, 0).bitcast(fp32), dest(kind, j, s, 1)
                    if kind in ("q", "k"):
                        bias, layer = {"q": bq_sb, "k": bk_sb}[kind], s // 2 % L
                        nc.vector.scalar_tensor_tensor(out=low, in0=bank_as(n, kind), scalar=bias[:, layer:layer + 1],
                                                       in1=high, op0=ALU.add, op1=ALU.subtract).then_inc(proj_split, 1)
                    else:
                        nc.vector.tensor_tensor(low, bank_as(n, kind), high, ALU.subtract).then_inc(proj_split, 1)

            def context_part(p, u):
                r = u % RING
                dve.wait_ge(ctx_made, p * STEPS + (u + 1))
                dve.wait_ge(weighted, p * STEPS + (u + 1))
                if u >= RING:
                    dve.wait_ge(nodes_made, p * STEPS + (u - RING + 1))
                nc.vector.scalar_tensor_tensor(out=part[:, :], in0=ctx_ps[u % 2][:, D:2 * D],
                                               scalar=weight[:, r:r + 1],
                                               in1=nodes[u // TILES % 2][:, u % TILES, :],
                                               op0=ALU.mult, op1=ALU.add).then_inc(part_made, 1)

            def transposed_low(p, v):
                for h in range(2):
                    dve.wait_ge(pT_high, p * (2 * STEPS) + (2 * v + h + 1))
                    nc.vector.tensor_tensor(pT[v % 2][1][:, 4 * h:4 * h + 4, :],
                                            pT_ps[:, BANK * h:BANK * (h + 1)].rearrange("p (a c) -> p a c", c=P),
                                            pT[v % 2][0][:, 4 * h:4 * h + 4, :].bitcast(fp32),
                                            ALU.subtract).then_inc(pT_split, 1)

            def step(p, last, g):
                s, t = g // TILES, g % TILES
                u, v = g - 3, g - 2
                if exists(p, last, v) and s == STAGES and last:
                    transposed_low(p, v)
                if exists(p, last, u):
                    context_part(p, u)
                if exists(p, last, v) and not (s == STAGES and last):
                    transposed_low(p, v)
                if exists(p, last, u):
                    r = u % RING
                    dve.wait_ge(part_made, p * STEPS + (u + 1))
                    nc.vector.scalar_tensor_tensor(out=y[:, r, :], in0=ctx_ps[u % 2][:, 0:D],
                                                   scalar=weight[:, r:r + 1], in1=part[:, :],
                                                   op0=ALU.mult, op1=ALU.add).then_inc(y_made, 1)
                if exists(p, last, g):
                    if s == 0:
                        dve.wait_ge((early_penalties, penalties)[t % 2], t // 2 + 1)
                    elif t == 0 and s % STAGES < 2:
                        if s == 1:
                            dve.wait_ge(early_penalties, EARLY)
                        dve.wait_ge(penalties, p * 16 + (16 * (s // STAGES) + 8 * (s % STAGES + 1) - EARLY))
                    dve.wait_ge(scores_made, p * STEPS + (g + 1))
                if exists(p, last, v):
                    r = v % RING
                    nc.vector.reciprocal(inverse[:, r:r + 1], row_sum[:, r:r + 1]).then_inc(inverted, 1)
                if exists(p, last, g):
                    r = g % RING
                    nc.vector.tensor_tensor_reduce(out=probs[g % 2][:, :], in0=scores_ps[:, :],
                                                   in1=penalty[s % 2][:, t, :], scale=-1.0 / SCALE, scalar=3e38,
                                                   op0=ALU.add, op1=ALU.min,
                                                   accum_out=neg_max[:, r:r + 1]).then_inc(masked, 1)
                if exists(p, last, v):
                    r = v % RING
                    dve.wait_ge(inverted, p * STEPS + (v + 1))
                    nc.vector.tensor_scalar(weight[:, r:r + 1], neg_max[:, r:r + 1], NO_EDGE,
                                            inverse[:, r:r + 1], ALU.is_lt, ALU.mult).then_inc(weighted, 1)
                if exists(p, last, u):
                    r = u % RING
                    dve.wait_ge(y_made, p * STEPS + (u + 1))
                    nc.vector.bn_stats(stats[:, r, :], y[:, r, :]).then_inc(stats_made, 1)
                if s == 0:
                    make_penalty(nc.vector, dve.wait_ge, p, 2 * t + 1, penalties)
                if s in (3, 4) and not last:
                    make_penalty(nc.vector, dve.wait_ge, p, 2 * TILES + TILES * (s - 3) + t, penalties)
                if exists(p, last, u):
                    dve.wait_ge(stats_made, p * STEPS + (u + 1))
                groups = groups_of(last, g)
                projections(p, groups[:1])
                if exists(p, last, u):
                    r = u % RING
                    nc.vector.bn_aggr(moments[:, r, :], stats[:, r, :]).then_inc(moments_made, 1)
                projections(p, groups[1:])
            projections(0, AHEAD_GROUPS[:FIRST_Q])
            dve.wait_ge(biases_in, 32)
            projections(0, AHEAD_GROUPS[FIRST_Q:])
            for g in FIRST:
                step(0, False, g)
            with dve.Fori(0, PAIRS - 1) as p:
                for g in BODY:
                    step(p, False, g)
            for g in BODY:
                step(PAIRS - 1, True, g)

            for i in range(2):
                r, t = (STEPS - 2 + i) % RING, TILES - 2 + i
                dve.wait_ge(last_rstd_made, i + 1)
                nc.vector.tensor_scalar(y[:, r, :], y[:, r, :], moments[:, r, 0:1], last_rstd[:, i:i + 1],
                                        ALU.subtract, ALU.mult).then_inc(last_norm_step, 1)
                dve.wait_ge(vectors_in, 32)
                dve.wait_ge(last_norm_step, 2 * i + 1)
                nc.vector.tensor_tensor(y[:, r, :], y[:, r, :], gain[:, L - 1, :],
                                        ALU.mult).then_inc(last_norm_step, 1)
                dve.wait_ge(last_norm_step, 2 * i + 2)
                nc.vector.tensor_tensor(nodes[1][:, t, :], y[:, r, :], shift[:, L - 1, :],
                                        ALU.add).then_inc(last_tiles_made, 1)

        @block.tensor
        def _(pe):
            def product(ps, terms):
                for i, (a, b) in enumerate(terms):
                    last = nc.tensor.matmul(ps, a, b, start=i == 0, stop=i == len(terms) - 1)
                return last

            def three(high_low_a, high_low_b):
                (ah, al), (bh, bl) = high_low_a, high_low_b
                return [(ah, bh), (ah, bl), (al, bh)]

            def projection(p, last, kind, j, s, n):
                layer, side = s // 2 % L, s % 2
                free = bank_free(n)
                if kind in ("q", "k"):
                    free = max(free, split_with(last, "xT", 2 * j + 1, s))
                if kind == "z":
                    free = max(free, split_with(last, "xT", j, s))
                if s == 0 and kind in ("q", "z"):
                    free = max(free, split_with(last, "wqk" if kind == "q" else "wc", 0, 0))
                if free > 0:
                    pe.wait_ge(proj_split, p * PAIR_GROUPS + free)
                if kind in ("wqk", "wc"):
                    if kind == "wqk":
                        pe.wait_ge(wqk_arrived[j], 32)
                    else:
                        pe.wait_ge(wc_arrived, 16 * L)
                    for a in range(2):
                        for d in range(DT):
                            src = (wq_in, wk_in)[a][:, j, d * P:(d + 1) * P] if kind == "wqk" else \
                                wc_in[:, j, a, d * P:(d + 1) * P]
                            at = (a * DT + d) * P if kind == "wqk" else d * D + a * P
                            done = nc.tensor.transpose(bank(n)[:, at:at + P], src, ident[:, :])
                elif kind == "xT":
                    if layer == 0:
                        pe.wait_ge(x_in[side][j], p * 16 + 16 * (s // STAGES + 1))
                    else:
                        pe.wait_ge(nodes_made, p * STEPS + (TILES * (s - 2) + 2 * j + 2))
                    for a in range(2):
                        for d in range(DT):
                            done = nc.tensor.transpose(bank_as(n, kind)[:, d, a * P:(a + 1) * P],
                                                       nodes[side][:, 2 * j + a, d * P:(d + 1) * P], ident[:, :])
                elif kind == "z":
                    high_low_w = wcT[layer]
                    for a in range(2):
                        c = (2 * j + a) * P
                        done = product(bank(n)[:, a * D:(a + 1) * D],
                                       [pair for d in range(DT)
                                        for pair in three([part[:, d, c:c + P] for part in xT],
                                                          [part[:, d, :] for part in high_low_w])])
                else:
                    m = 0 if kind == "q" else 1
                    done = product(bank(n)[:, :],
                                   [pair for d in range(DT)
                                    for pair in three([part[:, m, d * F:(d + 1) * F] for part in wqk[layer]],
                                                      [part[:, d, HALF * j:HALF * (j + 1)] for part in xT])])
                done.then_inc(proj_made, 1)

            def step(p, last, g):
                s, t = g // TILES, g % TILES
                side = s % 2
                if exists(p, last, g):
                    if t == 0:
                        pe.wait_ge(proj_split, p * PAIR_GROUPS + max(split_with(last, "k", 1, s),
                                                                     split_with(last, "q", int(g > 0), s)))
                    if g == TILES // 2:
                        pe.wait_ge(proj_split, split_with(last, "q", 1, 0))
                    if g > 0:
                        pe.wait_ge(masked, p * STEPS + g)
                    rows = slice(t * P, (t + 1) * P)
                    (qh, ql), (kh, kl) = q[side], k[side]
                    halves = [(scores_ps[:, HALF * h:HALF * (h + 1)], slice(HALF * h, HALF * (h + 1)))
                              for h in range(2)]
                    for ps, cols in halves:
                        nc.tensor.matmul(ps, qh[:, rows], kh[:, cols], start=True, stop=False)
                        nc.tensor.matmul(ps, qh[:, rows], kl[:, cols], start=False, stop=False)
                    for ps, cols in halves:
                        done = nc.tensor.matmul(ps, ql[:, rows], kh[:, cols], start=False, stop=True)
                    done.then_inc(scores_made, 1)
                for group in groups_of(last, g):
                    projection(p, last, *group)
                v = g - 1
                if exists(p, last, v):
                    pe.wait_ge(probs_made, p * STEPS + (v + 1))
                    for i in range(TILES):
                        if i % 4 == 0 and v > 0:
                            pe.wait_ge(pT_split, p * (2 * STEPS) + (2 * (v - 1) + i // 4 + 1))
                        done = nc.tensor.transpose(pT_ps[:, i * P:(i + 1) * P],
                                                   probs[v % 2][:, i * P:(i + 1) * P], ident[:, :])
                        if i % 4 == 3:
                            done.then_inc(pT_made, 1)
                u = g - 2
                if exists(p, last, u):
                    if u % TILES == 0:
                        pe.wait_ge(proj_split, p * PAIR_GROUPS + split_with(last, "z", 3, u // TILES))
                    zz, ps = z[u // TILES % 2], ctx_ps[u % 2]
                    pe.wait_ge(pT_split, p * (2 * STEPS) + (2 * u + 2))
                    (high, low) = pT[u % 2]
                    for i in range(TILES):
                        nc.tensor.matmul(ps[:, :], high[:, i, :], zz[:, i, :, :].rearrange("p a d -> p (a d)"),
                                         start=i == 0, stop=False)
                        done = nc.tensor.matmul(ps[:, 0:D], low[:, i, :], zz[:, i, 0, :],
                                                start=False, stop=i == TILES - 1)
                    done.then_inc(ctx_made, 1)

            pe.wait_ge(constants, 2)
            for _ in range(WARM_UP):
                nc.tensor.matmul(scores_ps[:, 0:P], ident[:, :], ident[:, :], start=True, stop=True)
            for group in AHEAD_GROUPS:
                projection(0, False, *group)
            for g in FIRST:
                step(0, False, g)
            with pe.Fori(0, PAIRS - 1) as p:
                for g in BODY:
                    step(p, False, g)
            for g in BODY:
                step(PAIRS - 1, True, g)


_INS = ['x', 'adj', 'L0_gnn_Wq', 'L0_gnn_bq', 'L0_gnn_Wk', 'L0_gnn_bk', 'L0_gnn_Wc', 'L0_gnn_ln_g', 'L0_gnn_ln_b']


def kernel(**inputs):
    import numpy as _np
    import concourse.bacc as _bacc
    from concourse import mybir as _mybir
    from concourse.bass_utils import run_bass_kernel_spmd as _run

    nc = _bacc.Bacc("TRN2", target_bir_lowering=False, num_devices=1)
    arrays, args = {}, []
    for name in _INS:
        a = _np.ascontiguousarray(inputs[name])
        arrays[f"in_{name}"] = a
        args.append(nc.dram_tensor(f"in_{name}", a.shape, _mybir.dt.from_np(a.dtype), kind="ExternalInput").ap())
    args.append(nc.dram_tensor("out_0", inputs["x"].shape, _mybir.dt.float32, kind="ExternalOutput").ap())
    gnn_kernel(nc, *args)
    r = _run(nc, [arrays], core_ids=[0])
    return r.results[0]["out_0"]
```
